# Optimizing a Trainium2 kernel written in Bass

```python
import numpy as np
import jax
import jax.numpy as jnp

def _softmax(x, axis=-1):
    return jax.nn.softmax(x, axis=axis)

def _gelu(x):
    return jax.nn.gelu(x, approximate=True)

def _silu(x):
    return jax.nn.silu(x)

def _sigmoid(x):
    return jax.nn.sigmoid(x)

def _layernorm(x, axis=-1, eps=1e-05):
    m = jnp.mean(x, axis=axis, keepdims=True)
    v = jnp.var(x, axis=axis, keepdims=True)
    return (x - m) / jnp.sqrt(v + eps)

def _scatter_add(tgt, idx, src, axis=0):
    return tgt.at[idx].add(src)

def _segment_sum(src, seg, n):
    return jax.ops.segment_sum(src, seg, n)
kernel_name = 'mk_xattn_seq_d2_seqx_r4_96d7f4'

def setup_inputs(seed: int=0):
    np.random.seed(seed)
    _w = jnp.asarray

    def _rec_inputs():
        import jax
        import jax.numpy as jnp
        _rk = jax.random.key(seed)
        x = -0.000125 + 0.9999 * jax.random.normal(jax.random.fold_in(_rk, 1), (8, 256, 512), jnp.float32)
        _lenS = 256 - jax.random.randint(jax.random.fold_in(_rk, 7), (8,), 0, max(1, 256 // 4) + 1, jnp.int32)
        _lenS2 = 256 - jax.random.randint(jax.random.fold_in(_rk, 8), (8,), 0, max(1, 256 // 4) + 1, jnp.int32)
        _ctx_2048P = jax.random.normal(jax.random.fold_in(_rk, 11), (8, 16, 512), jnp.float32)
        _ctx_2048c = jax.random.dirichlet(jax.random.fold_in(_rk, 511), 0.3 * jnp.ones((16,), jnp.float32), (8, 256))
        _ctx_2048t = jnp.einsum('bsk,bkd->bsd', _ctx_2048c, _ctx_2048P)
        _ctx_2048t = _ctx_2048t * jax.lax.rsqrt(jnp.mean(jnp.square(_ctx_2048t)) + 1e-12) * 0.953939
        ctx_2048 = -1.52775e-05 + 0.999936 * (_ctx_2048t + 0.3 * jax.random.normal(jax.random.fold_in(_rk, 611), (8, 256, 512), jnp.float32))
        return (x, ctx_2048)
    x, ctx_2048 = _rec_inputs()

    def _L0_xattn_setup():
        import jax, jax.numpy as jnp
        import numpy as np
        B, C, CI, N = (16, 256, 128, 512)
        EPS = 1e-05

        def _conv1x1(w, b, x):
            return jnp.einsum('oc,bcn->bon', w, x) + b[None, :, None]
        key = jax.random.key(seed)
        ks = jax.random.split(key, 14)
        s = 0.02
        return {'x': jax.random.normal(ks[0], (B, C, N), jnp.float32), 'x_2': jax.random.normal(ks[1], (B, C, N), jnp.float32), 'theta_w': jax.random.normal(ks[2], (CI, C), jnp.float32) * s, 'theta_b': jax.random.normal(ks[3], (CI,), jnp.float32) * s, 'phi_w': jax.random.normal(ks[4], (CI, C), jnp.float32) * s, 'phi_b': jax.random.normal(ks[5], (CI,), jnp.float32) * s, 'g_w': jax.random.normal(ks[6], (CI, C), jnp.float32) * s, 'g_b': jax.random.normal(ks[7], (CI,), jnp.float32) * s, 'w_w': jax.random.normal(ks[8], (C, CI), jnp.float32) * s, 'w_b': jax.random.normal(ks[9], (C,), jnp.float32) * s, 'bn_gamma': jax.random.normal(ks[10], (C,), jnp.float32), 'bn_beta': jax.random.normal(ks[11], (C,), jnp.float32), 'bn_mean': jax.random.normal(ks[12], (C,), jnp.float32), 'bn_var': jax.random.uniform(ks[13], (C,), jnp.float32, 0.5, 1.5)}
    _L0_xattn_all = _L0_xattn_setup()
    _L0_xattn_in = {k: v for k, v in _L0_xattn_all.items() if k in ('theta_w', 'theta_b', 'phi_w', 'phi_b', 'g_w', 'g_b', 'w_w', 'w_b', 'bn_gamma', 'bn_beta', 'bn_mean', 'bn_var')}
    del _L0_xattn_all

    def _L1_xattn_setup():
        import jax, jax.numpy as jnp
        import numpy as np
        N_HEAD = 32
        EPS = 1e-05

        def _ln(x, w, b):
            m = jnp.mean(x, axis=-1, keepdims=True)
            v = jnp.mean((x - m) ** 2, axis=-1, keepdims=True)
            return (x - m) * jax.lax.rsqrt(v + EPS) * w + b

        def _forward(x, state, i, ln1_w, ln1_b, ln2_w, ln2_b, maa_x, maa_w, maa_k, maa_v, maa_r, maa_g, maa_w1, maa_w2, time_decay, decay_w1, decay_w2, faaaa, Wr, Wk, Wv, Wg, Wo, gn_w, gn_b, fmaa_k, fmaa_r, fWk, fWr, fWv):
            B, L, C = x.shape
            H = N_HEAD
            S = C // H
            i0 = (2 + S) * i
            xa = _ln(x, ln1_w, ln1_b)
            sx = jnp.concatenate([state[:, i0 + 1][:, None], xa[:, :-1]], axis=1) - xa
            xxx = xa + sx * maa_x
            t = jnp.tanh(xxx @ maa_w1).reshape(B, L, 5, -1)
            m = jnp.einsum('blfd,fdc->blfc', t, maa_w2)
            mw, mk, mv, mr, mg = (m[:, :, j] for j in range(5))
            xw = xa + sx * (maa_w + mw)
            xk = xa + sx * (maa_k + mk)
            xv = xa + sx * (maa_v + mv)
            xr = xa + sx * (maa_r + mr)
            xg = xa + sx * (maa_g + mg)
            w = time_decay + jnp.tanh(xw @ decay_w1) @ decay_w2
            w = jnp.exp(-jnp.exp(w)).reshape(B, L, H, S)
            r = (xr @ Wr.T).reshape(B, L, H, S)
            k = (xk @ Wk.T).reshape(B, L, H, S)
            v = (xv @ Wv.T).reshape(B, L, H, S)
            g = jax.nn.silu(xg @ Wg.T)
            s0 = state[:, i0 + 2:i0 + 2 + S].reshape(B, H, S, S)

            def step(s, inp):
                k_l, v_l, w_l, r_l = inp
                a = k_l[..., :, None] * v_l[..., None, :]
                out = jnp.einsum('bhs,bhst->bht', r_l, faaaa * a + s)
                s_new = a + w_l[..., None] * s
                return (s_new, out)
            seq = tuple((z.transpose(1, 0, 2, 3) for z in (k, v, w, r)))
            _, outs = jax.lax.scan(step, s0, seq)
            y = outs.transpose(1, 0, 2, 3)
            gm = jnp.mean(y, axis=-1, keepdims=True)
            gv = jnp.mean((y - gm) ** 2, axis=-1, keepdims=True)
            y = ((y - gm) * jax.lax.rsqrt(gv + EPS)).reshape(B, L, C) * gn_w + gn_b
            x = x + y * g @ Wo.T
            xc = _ln(x, ln2_w, ln2_b)
            sxc = jnp.concatenate([state[:, i0][:, None], xc[:, :-1]], axis=1) - xc
            xk2 = xc + sxc * fmaa_k
            xr2 = xc + sxc * fmaa_r
            rr = jax.nn.sigmoid(xr2 @ fWr.T)
            kk = jnp.square(jax.nn.relu(xk2 @ fWk.T))
            x = x + rr * (kk @ fWv.T)
            return x
        key = jax.random.key(seed)
        B, L, C, H = (8, 128, 512, N_HEAD)
        S = C // H
        DM, DD = (32, 64)
        ks = jax.random.split(key, 32)
        n = lambda k, shp, s=1.0: jax.random.normal(k, shp, dtype=jnp.float32) * s
        u = lambda k, shp: jax.random.uniform(k, shp, dtype=jnp.float32)
        inp = {'x': n(ks[0], (B, L, C)), 'state': n(ks[1], (B, 2 + S, C), 0.1), 'i': 0, 'ln1_w': jnp.ones((C,), jnp.float32), 'ln1_b': jnp.zeros((C,), jnp.float32), 'ln2_w': jnp.ones((C,), jnp.float32), 'ln2_b': jnp.zeros((C,), jnp.float32), 'maa_x': u(ks[2], (C,)), 'maa_w': u(ks[3], (C,)), 'maa_k': u(ks[4], (C,)), 'maa_v': u(ks[5], (C,)), 'maa_r': u(ks[6], (C,)), 'maa_g': u(ks[7], (C,)), 'maa_w1': n(ks[8], (C, 5 * DM), 0.02), 'maa_w2': n(ks[9], (5, DM, C), 0.02), 'time_decay': n(ks[10], (C,), 0.5), 'decay_w1': n(ks[11], (C, DD), 0.02), 'decay_w2': n(ks[12], (DD, C), 0.02), 'faaaa': n(ks[13], (H, S, 1), 0.1), 'Wr': n(ks[14], (C, C), 0.02), 'Wk': n(ks[15], (C, C), 0.02), 'Wv': n(ks[16], (C, C), 0.02), 'Wg': n(ks[17], (C, C), 0.02), 'Wo': n(ks[18], (C, C), 0.02), 'gn_w': jnp.ones((C,), jnp.float32), 'gn_b': jnp.zeros((C,), jnp.float32), 'fmaa_k': u(ks[19], (C,)), 'fmaa_r': u(ks[20], (C,)), 'fWk': n(ks[21], (C, C), 0.02), 'fWr': n(ks[22], (C, C), 0.02), 'fWv': n(ks[23], (C, C), 0.02)}
        return inp
    _L1_xattn_all = _L1_xattn_setup()
    _L1_xattn_in = {k: v for k, v in _L1_xattn_all.items() if k in ('ln1_w', 'ln1_b', 'ln2_w', 'ln2_b', 'maa_x', 'maa_w', 'maa_k', 'maa_v', 'maa_r', 'maa_g', 'maa_w1', 'maa_w2', 'time_decay', 'decay_w1', 'decay_w2', 'faaaa', 'Wr', 'Wk', 'Wv', 'Wg', 'Wo', 'gn_w', 'gn_b', 'fmaa_k', 'fmaa_r', 'fWk', 'fWr', 'fWv')}
    del _L1_xattn_all
    return {'x': x, 'ctx_2048': ctx_2048, 'L0_xattn_theta_w': _L0_xattn_in['theta_w'], 'L0_xattn_theta_b': _L0_xattn_in['theta_b'], 'L0_xattn_phi_w': _L0_xattn_in['phi_w'], 'L0_xattn_phi_b': _L0_xattn_in['phi_b'], 'L0_xattn_g_w': _L0_xattn_in['g_w'], 'L0_xattn_g_b': _L0_xattn_in['g_b'], 'L0_xattn_w_w': _L0_xattn_in['w_w'], 'L0_xattn_w_b': _L0_xattn_in['w_b'], 'L0_xattn_bn_gamma': _L0_xattn_in['bn_gamma'], 'L0_xattn_bn_beta': _L0_xattn_in['bn_beta'], 'L0_xattn_bn_mean': _L0_xattn_in['bn_mean'], 'L0_xattn_bn_var': _L0_xattn_in['bn_var'], 'L1_xattn_ln1_w': _L1_xattn_in['ln1_w'], 'L1_xattn_ln1_b': _L1_xattn_in['ln1_b'], 'L1_xattn_ln2_w': _L1_xattn_in['ln2_w'], 'L1_xattn_ln2_b': _L1_xattn_in['ln2_b'], 'L1_xattn_maa_x': _L1_xattn_in['maa_x'], 'L1_xattn_maa_w': _L1_xattn_in['maa_w'], 'L1_xattn_maa_k': _L1_xattn_in['maa_k'], 'L1_xattn_maa_v': _L1_xattn_in['maa_v'], 'L1_xattn_maa_r': _L1_xattn_in['maa_r'], 'L1_xattn_maa_g': _L1_xattn_in['maa_g'], 'L1_xattn_maa_w1': _L1_xattn_in['maa_w1'], 'L1_xattn_maa_w2': _L1_xattn_in['maa_w2'], 'L1_xattn_time_decay': _L1_xattn_in['time_decay'], 'L1_xattn_decay_w1': _L1_xattn_in['decay_w1'], 'L1_xattn_decay_w2': _L1_xattn_in['decay_w2'], 'L1_xattn_faaaa': _L1_xattn_in['faaaa'], 'L1_xattn_Wr': _L1_xattn_in['Wr'], 'L1_xattn_Wk': _L1_xattn_in['Wk'], 'L1_xattn_Wv': _L1_xattn_in['Wv'], 'L1_xattn_Wg': _L1_xattn_in['Wg'], 'L1_xattn_Wo': _L1_xattn_in['Wo'], 'L1_xattn_gn_w': _L1_xattn_in['gn_w'], 'L1_xattn_gn_b': _L1_xattn_in['gn_b'], 'L1_xattn_fmaa_k': _L1_xattn_in['fmaa_k'], 'L1_xattn_fmaa_r': _L1_xattn_in['fmaa_r'], 'L1_xattn_fWk': _L1_xattn_in['fWk'], 'L1_xattn_fWr': _L1_xattn_in['fWr'], 'L1_xattn_fWv': _L1_xattn_in['fWv']}

def reference(x, ctx_2048, L0_xattn_theta_w, L0_xattn_theta_b, L0_xattn_phi_w, L0_xattn_phi_b, L0_xattn_g_w, L0_xattn_g_b, L0_xattn_w_w, L0_xattn_w_b, L0_xattn_bn_gamma, L0_xattn_bn_beta, L0_xattn_bn_mean, L0_xattn_bn_var, L1_xattn_ln1_w, L1_xattn_ln1_b, L1_xattn_ln2_w, L1_xattn_ln2_b, L1_xattn_maa_x, L1_xattn_maa_w, L1_xattn_maa_k, L1_xattn_maa_v, L1_xattn_maa_r, L1_xattn_maa_g, L1_xattn_maa_w1, L1_xattn_maa_w2, L1_xattn_time_decay, L1_xattn_decay_w1, L1_xattn_decay_w2, L1_xattn_faaaa, L1_xattn_Wr, L1_xattn_Wk, L1_xattn_Wv, L1_xattn_Wg, L1_xattn_Wo, L1_xattn_gn_w, L1_xattn_gn_b, L1_xattn_fmaa_k, L1_xattn_fmaa_r, L1_xattn_fWk, L1_xattn_fWr, L1_xattn_fWv):
    import jax
    import jax.numpy as jnp

    def _L0_xattn_ref(x, x_2, theta_w, theta_b, phi_w, phi_b, g_w, g_b, w_w, w_b, bn_gamma, bn_beta, bn_mean, bn_var):
        import jax, jax.numpy as jnp
        import numpy as np
        B, C, CI, N = (16, 256, 128, 512)
        EPS = 1e-05

        def _conv1x1(w, b, x):
            return jnp.einsum('oc,bcn->bon', w, x) + b[None, :, None]
        g_x = _conv1x1(g_w, g_b, x_2).transpose(0, 2, 1)
        theta_x = _conv1x1(theta_w, theta_b, x).transpose(0, 2, 1)
        phi_x = _conv1x1(phi_w, phi_b, x_2)
        W = jnp.einsum('bnc,bcm->bnm', theta_x, phi_x) / phi_x.shape[-1]
        y = jnp.einsum('bnm,bmc->bnc', W, g_x).transpose(0, 2, 1)
        wy = _conv1x1(w_w, w_b, y)
        inv_std = jax.lax.rsqrt(bn_var + EPS)
        wy = bn_gamma[None, :, None] * (wy - bn_mean[None, :, None]) * inv_std[None, :, None] + bn_beta[None, :, None]
        return wy + x

    def _L1_xattn_ref(x, state, i, ln1_w, ln1_b, ln2_w, ln2_b, maa_x, maa_w, maa_k, maa_v, maa_r, maa_g, maa_w1, maa_w2, time_decay, decay_w1, decay_w2, faaaa, Wr, Wk, Wv, Wg, Wo, gn_w, gn_b, fmaa_k, fmaa_r, fWk, fWr, fWv):
        import jax, jax.numpy as jnp
        import numpy as np
        N_HEAD = 32
        EPS = 1e-05

        def _ln(x, w, b):
            m = jnp.mean(x, axis=-1, keepdims=True)
            v = jnp.mean((x - m) ** 2, axis=-1, keepdims=True)
            return (x - m) * jax.lax.rsqrt(v + EPS) * w + b

        def _forward(x, state, i, ln1_w, ln1_b, ln2_w, ln2_b, maa_x, maa_w, maa_k, maa_v, maa_r, maa_g, maa_w1, maa_w2, time_decay, decay_w1, decay_w2, faaaa, Wr, Wk, Wv, Wg, Wo, gn_w, gn_b, fmaa_k, fmaa_r, fWk, fWr, fWv):
            B, L, C = x.shape
            H = N_HEAD
            S = C // H
            i0 = (2 + S) * i
            xa = _ln(x, ln1_w, ln1_b)
            sx = jnp.concatenate([state[:, i0 + 1][:, None], xa[:, :-1]], axis=1) - xa
            xxx = xa + sx * maa_x
            t = jnp.tanh(xxx @ maa_w1).reshape(B, L, 5, -1)
            m = jnp.einsum('blfd,fdc->blfc', t, maa_w2)
            mw, mk, mv, mr, mg = (m[:, :, j] for j in range(5))
            xw = xa + sx * (maa_w + mw)
            xk = xa + sx * (maa_k + mk)
            xv = xa + sx * (maa_v + mv)
            xr = xa + sx * (maa_r + mr)
            xg = xa + sx * (maa_g + mg)
            w = time_decay + jnp.tanh(xw @ decay_w1) @ decay_w2
            w = jnp.exp(-jnp.exp(w)).reshape(B, L, H, S)
            r = (xr @ Wr.T).reshape(B, L, H, S)
            k = (xk @ Wk.T).reshape(B, L, H, S)
            v = (xv @ Wv.T).reshape(B, L, H, S)
            g = jax.nn.silu(xg @ Wg.T)
            s0 = state[:, i0 + 2:i0 + 2 + S].reshape(B, H, S, S)

            def step(s, inp):
                k_l, v_l, w_l, r_l = inp
                a = k_l[..., :, None] * v_l[..., None, :]
                out = jnp.einsum('bhs,bhst->bht', r_l, faaaa * a + s)
                s_new = a + w_l[..., None] * s
                return (s_new, out)
            seq = tuple((z.transpose(1, 0, 2, 3) for z in (k, v, w, r)))
            _, outs = jax.lax.scan(step, s0, seq)
            y = outs.transpose(1, 0, 2, 3)
            gm = jnp.mean(y, axis=-1, keepdims=True)
            gv = jnp.mean((y - gm) ** 2, axis=-1, keepdims=True)
            y = ((y - gm) * jax.lax.rsqrt(gv + EPS)).reshape(B, L, C) * gn_w + gn_b
            x = x + y * g @ Wo.T
            xc = _ln(x, ln2_w, ln2_b)
            sxc = jnp.concatenate([state[:, i0][:, None], xc[:, :-1]], axis=1) - xc
            xk2 = xc + sxc * fmaa_k
            xr2 = xc + sxc * fmaa_r
            rr = jax.nn.sigmoid(xr2 @ fWr.T)
            kk = jnp.square(jax.nn.relu(xk2 @ fWk.T))
            x = x + rr * (kk @ fWv.T)
            return x
        return _forward(x, state, i, ln1_w, ln1_b, ln2_w, ln2_b, maa_x, maa_w, maa_k, maa_v, maa_r, maa_g, maa_w1, maa_w2, time_decay, decay_w1, decay_w2, faaaa, Wr, Wk, Wv, Wg, Wo, gn_w, gn_b, fmaa_k, fmaa_r, fWk, fWr, fWv)
    x = _L0_xattn_ref(x, ctx_2048, L0_xattn_theta_w, L0_xattn_theta_b, L0_xattn_phi_w, L0_xattn_phi_b, L0_xattn_g_w, L0_xattn_g_b, L0_xattn_w_w, L0_xattn_w_b, L0_xattn_bn_gamma, L0_xattn_bn_beta, L0_xattn_bn_mean, L0_xattn_bn_var)
    x = _L1_xattn_ref(x, ctx_2048, 0, L1_xattn_ln1_w, L1_xattn_ln1_b, L1_xattn_ln2_w, L1_xattn_ln2_b, L1_xattn_maa_x, L1_xattn_maa_w, L1_xattn_maa_k, L1_xattn_maa_v, L1_xattn_maa_r, L1_xattn_maa_g, L1_xattn_maa_w1, L1_xattn_maa_w2, L1_xattn_time_decay, L1_xattn_decay_w1, L1_xattn_decay_w2, L1_xattn_faaaa, L1_xattn_Wr, L1_xattn_Wk, L1_xattn_Wv, L1_xattn_Wg, L1_xattn_Wo, L1_xattn_gn_w, L1_xattn_gn_b, L1_xattn_fmaa_k, L1_xattn_fmaa_r, L1_xattn_fWk, L1_xattn_fWr, L1_xattn_fWv)
    return x

_drawn_inputs = setup_inputs


def setup_inputs(seed=0):
    import zlib

    import numpy as np

    out = dict(_drawn_inputs(seed))
    spreads = {'L1_xattn_ln1_w': (1.0, 0.6),
     'L1_xattn_ln1_b': (0.0, 2.0),
     'L1_xattn_ln2_w': (1.0, 0.6),
     'L1_xattn_ln2_b': (0.0, 2.0),
     'L1_xattn_gn_w': (1.0, 0.6),
     'L1_xattn_gn_b': (0.0, 2.0)}
    factors = {'ctx_2048': 4.729,
     'L0_xattn_theta_w': 3.369,
     'L0_xattn_theta_b': 8.0,
     'L0_xattn_phi_w': 3.234,
     'L0_xattn_phi_b': 64.0,
     'L0_xattn_g_w': 3.415,
     'L0_xattn_g_b': 64.0,
     'L0_xattn_w_w': 3.169,
     'L0_xattn_w_b': 200.0,
     'L1_xattn_maa_x': 43.205,
     'L1_xattn_maa_w': 64.0,
     'L1_xattn_maa_w1': 27.351,
     'L1_xattn_maa_w2': 28.465,
     'L1_xattn_time_decay': 23.576,
     'L1_xattn_decay_w1': 64.0,
     'L1_xattn_decay_w2': 64.0,
     'L1_xattn_faaaa': 52.848,
     'L1_xattn_fmaa_k': 4.629,
     'L1_xattn_fmaa_r': 8.0,
     'L1_xattn_fWk': 2.675,
     'L1_xattn_fWr': 8.0,
     'L0_xattn_bn_beta': 4.533,
     'L0_xattn_bn_mean': 4.438,
     'L1_xattn_maa_k': 8.0,
     'L1_xattn_maa_v': 8.0,
     'L1_xattn_maa_r': 8.0,
     'L1_xattn_maa_g': 8.0,
     'L1_xattn_Wr': 4.733,
     'L1_xattn_Wk': 5.174,
     'L1_xattn_Wv': 5.182,
     'L1_xattn_Wg': 4.495,
     'L1_xattn_Wo': 4.358}
    for name, (base, spread) in spreads.items():
        noise = np.random.default_rng([zlib.crc32(name.encode()), seed]).standard_normal(out[name].shape)
        drawn = base * np.exp(spread * noise) if base else spread * noise
        out[name] = jnp.asarray(drawn.astype(out[name].dtype))
    for name, factor in factors.items():
        out[name] = (out[name] * factor).astype(out[name].dtype)
    return out
```

```python
from contextlib import ExitStack

import concourse.bass as bass
from concourse import mybir
from concourse.alu_op_type import AluOpType as ALU

ACT = mybir.ActivationFunctionType
F32 = mybir.dt.float32
AX = mybir.AxisListType

P = 128
EPS = 1e-5
CHANNEL_VECTORS = ["ln1_w", "ln1_b", "ln2_w", "ln2_b", "maa_x", "maa_w", "maa_k", "maa_v", "maa_r", "maa_g",
                   "time_decay", "faaaa", "gn_w", "gn_b", "fmaa_k", "fmaa_r"]
BN_VECTORS = ["w_b", "bn_gamma", "bn_beta", "bn_mean", "bn_var"]
SQUARE = ["Wk", "Wv", "Wr", "Wg", "Wo", "fWk", "fWr", "fWv"]


def build_xattn_rwkv(nc, x_d, ctx_d, shift_d, chan_d, bnv_d, theta_b_d, pgb_d, thetaT_d, pgT_d, ww_d,
                     maa_w1_d, maa_w2_d, dec_w1_d, dec_w2_d, square_d, ident_d, ones16_d, sel_d, selT_d, out_d):
    B, L, C = x_d.shape
    S = 16
    CT = C // P
    TT = L // P
    F = CT * L
    CI = P
    DM, DD = 32, 64
    CHUNK = 512
    INTRA = [1, 2, 4, 8]
    STATES = [16, 32, 64, 128]
    DIAG = F // CHUNK
    N_CHUNKS = DIAG + sum(INTRA)
    GROUPS = [(h, tt, q) for h in STATES for tt in range(TT if h < P else 1) for q in range(0, P, 2 * h)]
    N_GROUPS = len(GROUPS)
    MIXES = ["w", "k", "v", "r", "g"]

    with ExitStack() as ctx:
        def sb(name, shape):
            return ctx.enter_context(nc.sbuf_tensor(name, shape, F32))

        def ps(name, shape):
            return ctx.enter_context(nc.psum_tensor(name, shape, F32))

        def sem(name):
            return ctx.enter_context(nc.semaphore(name))

        chan = sb("chan", [P, len(CHANNEL_VECTORS), CT])
        bnv = sb("bnv", [P, len(BN_VECTORS), TT])
        theta_b = sb("theta_b", [P, 1])
        pg_bias = sb("pg_bias", [P, 2 * CI])
        thetaT = sb("thetaT", [P, TT, CI])
        pgT = sb("pgT", [P, TT, 2 * CI])
        ww = sb("ww", [P, TT, CI])
        wwT = sb("wwT", [P, L])
        maa_w1 = sb("maa_w1", [P, CT, 5 * DM])
        maa_w2 = sb("maa_w2", [P, C])
        maa_w2g = sb("maa_w2g", [DM, C])
        dec_w1 = sb("dec_w1", [P, CT, DD])
        dec_w2 = sb("dec_w2", [DD, C])
        sq_w = {n: sb("sq_" + n, [P, CT, C]) for n in SQUARE}
        ident = sb("ident", [P, P])
        ones16 = sb("ones16", [P, P])
        sel = sb("sel", [P, CT, 32])
        selT = sb("selT", [32, CT, P])
        eps_c = sb("eps_c", [P, TT])
        eps32 = sb("eps32", [32, 1])
        neg_half = sb("neg_half", [P, TT])
        bn_s = sb("bn_s", [P, TT])
        bn_t = sb("bn_t", [P, TT])
        bn_tmp = sb("bn_tmp", [P, 2, TT])

        def vec(name, ct):
            i = CHANNEL_VECTORS.index(name)
            return chan[:, i, ct:ct + 1]

        x = sb("x", [P, TT, C])
        ctx_t = sb("ctx_t", [P, TT, C])
        zbuf = sb("zbuf", [P, F])
        theta = sb("theta", [P, C])
        att = sb("att", [P, CI])
        wa = sb("wa", [P, L])
        x1 = sb("x1", [P, TT, C])
        xres = sb("xres", [P, TT, C])
        stats = sb("stats", [P, TT, 6])
        mv = sb("mv", [P, TT, 2])
        rstd = sb("rstd", [P, TT])
        xa = sb("xa", [P, CT, L + 1])
        xa0 = sb("xa0", [P, CT])
        sx = sb("sx", [P, CT, L])
        tmix = sb("tmix", [P, L])
        tmix_g = sb("tmix_g", [DM, L])
        xmix = sb("xmix", [P, 2, CT, L])
        dec = sb("dec", [DD, L])
        W = sb("W", [P, F])
        K = sb("K", [P, F])
        RA = sb("RA", [P, F])
        vT = sb("vT", [P, F])
        vrow = sb("vrow", [P, TT, C])
        gate = sb("gate", [P, F])
        RB = sb("RB", [P, F])
        wprod = sb("wprod", [P, F])
        prod = sb("prod", [P, 3, CHUNK])
        av = sb("av", [P, 2, CHUNK])
        yred = sb("yred", [P, F // 2])
        yint = sb("yint", [P, F])
        krow = sb("krow", [P, 2, TT, C])
        S0 = sb("S0", [P, CT, P])
        St = sb("St", [P, 2, CT, P])
        y = sb("y", [P, F])
        sqb = sb("sqb", [P, F])
        gstd = sb("gstd", [32, L])
        grstd = sb("grstd", [32, L])
        x2 = sb("x2", [P, TT, C])
        stats2 = sb("stats2", [P, TT, 6])
        mv2 = sb("mv2", [P, TT, 2])
        rstd2 = sb("rstd2", [P, TT])
        xc = sb("xc", [P, CT, L + 1])
        xc0 = sb("xc0", [P, CT])
        sxc = yint[:].rearrange("p (c t) -> p c t", c=CT)
        xk2, xr2 = (krow[:, n].rearrange("p t c -> p (t c)").rearrange("p (c t) -> p c t", c=CT) for n in range(2))

        PA = ps("PA", [P, 1024])
        PB = ps("PB", [P, 1024])
        CH = ps("CH", [P, 1024])
        Y = ps("Y", [P, 1024])

        w_att, w_vec, w_mix, w_const = sem("w_att"), sem("w_vec"), sem("w_mix"), sem("w_const")
        w_sq = {n: sem("w_" + n) for n in SQUARE}
        const_set, pool_set, ww_scaled, ww_turned, bn_ready, wo_half, s0_zero = (
            sem(n) for n in ["const_set", "pool_set", "ww_scaled", "ww_turned", "bn_ready", "wo_half", "s0_zero"])
        wwT_ready = sem("wwT_ready")
        x_in, ctx_in, s0_in, xa0_in, xc0_in = (sem(n) for n in ["x_in", "ctx_in", "s0_in", "xa0_in", "xc0_in"])
        pg_mm, pg_ready, theta_mm, theta_ready, att_mm, att_ready, wa_mm, wa_ready = (
            sem(n) for n in ["pg_mm", "pg_ready", "theta_mm", "theta_ready", "att_mm", "att_ready", "wa_mm", "wa_ready"])
        x1_mm, x1_ready, bn1_stat, bn1_aggr, var1_eps, rstd1_ready, z1_ready, z1_turned, xa_ready = (
            sem(n) for n in ["x1_mm", "x1_ready", "bn1_stat", "bn1_aggr", "var1_eps", "rstd1_ready", "z1_ready",
                             "z1_turned", "xa_ready"])
        sx_ready, xxx_ready, rank_mm, tmix_ready = (sem(n) for n in ["sx_ready", "xxx_ready", "rank_mm", "tmix_ready"])
        mix_mm, mix_scaled, mix_ready, proj_mm = (sem(n) for n in ["mix_mm", "mix_scaled", "mix_ready", "proj_mm"])
        dec_mm, dec_ready, decay_exp, W_ready = (sem(n) for n in ["dec_mm", "dec_ready", "decay_exp", "W_ready"])
        K_ready, vT_ready, v_turned, vrow_ready, R_ready, gtanh_ready, gate_ready, xres_ready = (
            sem(n) for n in ["K_ready", "vT_ready", "v_turned", "vrow_ready", "R_ready", "gtanh_ready", "gate_ready",
                             "xres_ready"])
        wprod_ready = sem("wprod_ready")
        prod_ready = {"dve": sem("prod_dve"), "pool": sem("prod_pool")}
        chunk_mm = sem("chunk_mm")
        av_ready = sem("av_ready")
        red_ready = sem("red_ready")
        yint_ready = sem("yint_ready")
        R_up, K_up, R_kept = sem("R_up"), sem("K_up"), sem("R_kept")
        k_turned, krow_ready = sem("k_turned"), sem("krow_ready")
        st_mm, st_ready, st_read = sem("st_mm"), sem("st_ready"), sem("st_read")
        s1_masked, y_mm, y_ready = sem("s1_masked"), sem("y_mm"), sem("y_ready")
        mean_mm, d_ready, sq_ready, var_mm, gstd_ready, grstd_ready, grstd_mm, yn_ready, yg_ready = (
            sem(n) for n in ["mean_mm", "d_ready", "sq_ready", "var_mm", "gstd_ready", "grstd_ready", "grstd_mm",
                             "yn_ready", "yg_ready"])
        wo_mm, x2_ready, bn2_stat, bn2_aggr, var2_eps, rstd2_ready, z2_ready, z2_turned, xc_ready = (
            sem(n) for n in ["wo_mm", "x2_ready", "bn2_stat", "bn2_aggr", "var2_eps", "rstd2_ready", "z2_ready",
                             "z2_turned", "xc_ready"])
        sxc_ready, xk2_ready, xr2_ready, fk_mm, relu_ready, kk_ready, fr_mm, sig_ready, fv_mm, ff_scaled = (
            sem(n) for n in ["sxc_ready", "xk2_ready", "xr2_ready", "fk_mm", "relu_ready", "kk_ready", "fr_mm",
                             "sig_ready", "fv_mm", "ff_scaled"])
        out_ready, out_stored = sem("out_ready"), sem("out_stored")

        def at(b, n=1, k=None):
            return b * n + (n if k is None else k)

        def at_before(b, n=1, k=None):
            return b * n - n + (n if k is None else k)

        def later(b):
            return not (isinstance(b, int) and b == 0)

        def cols(t):
            return t.rearrange("p (c t) -> p c t", c=CT)

        CHUNKS = [(i, 0, i) for i in range(DIAG)]
        for h in INTRA:
            CHUNKS += [(len(CHUNKS) + i, h, i) for i in range(h)]
        POOL_CHUNKS = [g for g, h, c in CHUNKS if h > 1]
        DVE_CHUNKS = [g for g, h, c in CHUNKS if g not in POOL_CHUNKS]
        FIRST_CHUNK = {h: min(g for g, hh, c in CHUNKS if hh == h) for h in INTRA}

        def prod_signal(g):
            return ("pool", len(POOL_CHUNKS), POOL_CHUNKS.index(g) + 1) if g in POOL_CHUNKS else (
                "dve", len(DVE_CHUNKS), DVE_CHUNKS.index(g) + 1)

        def pairs(t, h, c, odd):
            nb = CHUNK // (h * h)
            v = t.rearrange("p (n two h) -> p n two h", two=2, h=h)
            return v[:, c * nb:(c + 1) * nb, odd, :]

        def by_pair(ap, h):
            return ap.rearrange("p (n i j) -> p n i j", i=h, j=h)

        def halves(t, h, odd):
            return t.rearrange("p (n two h) -> p n two h", two=2, h=h)[:, :, odd, :]

        WOFF = {}
        off = 0
        for h in [2, 4, 8, 16, 32, 64, 128]:
            WOFF[h] = off
            off += F // h

        def wblocks(h):
            t = W[:] if h == 1 else wprod[:, WOFF[h]:WOFF[h] + F // h]
            return t.rearrange("p (n two) -> p n two", two=2)

        def wfactor(h, odd):
            n = F // (2 * h)
            return wblocks(h)[:, :, odd:odd + 1].to_broadcast([P, n, h])

        R_OF = {16: RA, 32: RB, 64: RA, 128: RB}
        block = ctx.enter_context(nc.Block())

        @block.sync
        def _(sp):
            def load_x(b):
                if later(b):
                    sp.wait_ge(x1_ready, at_before(b, TT))
                sp.dma_start(x[:], x_d[b].rearrange("(t p) c -> p t c", p=P)).then_inc(x_in, 16)

            def load_ctx(b):
                if later(b):
                    sp.wait_ge(pg_mm, at_before(b))
                sp.dma_start(ctx_t[:], ctx_d[b].rearrange("(t p) c -> p t c", p=P)).then_inc(ctx_in, 16)

            def load_state(b):
                if later(b):
                    sp.wait_ge(y_mm, at_before(b))
                for g in range(P // S):
                    src = ctx_d[b, 2:2 + S, :].rearrange("r c -> (r c)").rearrange(
                        "(ct g s t) -> g s ct t", ct=CT, g=P // S, s=S)
                    sp.dma_start(S0[g * S:(g + 1) * S, :, g * S:(g + 1) * S], src[g]).then_inc(s0_in, 16)

            def load_xa0(b):
                if later(b):
                    sp.wait_ge(xa_ready, at_before(b))
                sp.dma_start(xa0[:], shift_d[b, 1]).then_inc(xa0_in, 16)

            def load_xc0(b):
                if later(b):
                    sp.wait_ge(xc_ready, at_before(b))
                sp.dma_start(xc0[:], shift_d[b, 0]).then_inc(xc0_in, 16)

            def store(b):
                sp.wait_ge(out_ready, at(b))
                sp.dma_start(out_d[b].rearrange("(t p) c -> p t c", p=P), x2[:]).then_inc(out_stored, 16)

            load_ctx(0)
            sp.dma_start(pgT[:], pgT_d.rearrange("(t p) c -> p t c", p=P)).then_inc(w_att, 16)
            sp.dma_start(pg_bias[:], pgb_d.partition_broadcast(P)).then_inc(w_att, 16)
            load_x(0)
            sp.dma_start(thetaT[:], thetaT_d.rearrange("(t p) c -> p t c", p=P)).then_inc(w_att, 16)
            sp.dma_start(theta_b[:], theta_b_d).then_inc(w_att, 16)
            load_xa0(0)
            for n in ["Wk", "Wv", "Wr", "Wg", "Wo", "fWk", "fWr", "fWv"]:
                sp.dma_start(sq_w[n][:], square_d[SQUARE.index(n)].rearrange("(t p) c -> p t c", p=P)).then_inc(w_sq[n], 16)
            load_ctx(1)
            load_x(1)
            load_xa0(1)
            sp.wait_ge(s0_zero, 1)
            load_state(0)
            load_xc0(0)
            load_ctx(2)
            load_x(2)
            load_xa0(2)
            load_state(1)
            load_ctx(3)
            load_xc0(1)
            load_x(3)
            load_xa0(3)
            with sp.Fori(2, B - 2) as i:
                store(i - 2)
                load_state(i)
                load_ctx(i + 2)
                load_xc0(i)
                load_x(i + 2)
                load_xa0(i + 2)
            for b in [B - 2, B - 1]:
                store(b - 2)
                load_state(b)
                load_xc0(b)
            store(B - 2)
            store(B - 1)
            sp.wait_ge(out_stored, 16 * B)

        @block.tensor
        def _(pe):
            def a_phi_g(b):
                pe.wait_ge(ctx_in, at(b, 16))
                if later(b):
                    pe.wait_ge(mix_scaled, at_before(b, 5))
                for m in range(CT):
                    for kt in range(TT):
                        mm = pe.matmul(PA[:, m * 256:(m + 1) * 256], ctx_t[:, kt, m * P:(m + 1) * P], pgT[:, kt, :],
                                       start=(kt == 0), stop=(kt == TT - 1))
                mm.then_inc(pg_mm, 1)

            def a_theta(b):
                pe.wait_ge(x_in, at(b, 16))
                if later(b):
                    pe.wait_ge(gate_ready, at_before(b))
                for kt in range(TT):
                    mm = pe.matmul(PB[:, 0:C], thetaT[:, kt, :], x[:, kt, :], start=(kt == 0), stop=(kt == TT - 1))
                mm.then_inc(theta_mm, 1)

            def a_att(b):
                pe.wait_ge(pg_ready, at(b))
                for m in range(CT):
                    mm = pe.matmul(PA[:, 0:CI], zbuf[:, m * 256 + CI:(m + 1) * 256], zbuf[:, m * 256:m * 256 + CI],
                                   start=(m == 0), stop=(m == CT - 1))
                mm.then_inc(att_mm, 1)

            def a_wa(b):
                pe.wait_ge(att_ready, at(b))
                pe.matmul(PA[:, 512:512 + L], att[:], wwT[:], start=True, stop=True).then_inc(wa_mm, 1)

            def a_x1(b):
                pe.wait_ge(theta_ready, at(b))
                pe.wait_ge(wa_ready, at(b))
                for t in range(TT):
                    pe.matmul(PA[:, t * C:(t + 1) * C], wa[:, t * P:(t + 1) * P], theta[:],
                              start=True, stop=True).then_inc(x1_mm, 1)

            def turn_rows(rows, out, signal):
                for ct in range(CT):
                    for t in range(TT):
                        mm = pe.transpose(out[:, ct * L + t * P:ct * L + (t + 1) * P],
                                          rows[:, t * C + ct * P:t * C + (ct + 1) * P], ident[:])
                mm.then_inc(signal, 1)

            def a_turn(b):
                pe.wait_ge(z1_ready, at(b))
                turn_rows(zbuf, PA, z1_turned)

            def a_ranks(b):
                pe.wait_ge(xxx_ready, at(b))
                pe.wait_ge(theta_ready, at(b))
                for lo, m, dst in [(0, P, PB[:, 512:768]), (P, DM, PB[0:DM, 768:1024])]:
                    for kt in range(CT):
                        mm = pe.matmul(dst, maa_w1[:, kt, lo:lo + m], zbuf[:, kt * L:(kt + 1) * L],
                                       start=(kt == 0), stop=(kt == CT - 1))
                mm.then_inc(rank_mm, 1)

            def a_mix(b, j):
                if j == 0:
                    pe.wait_ge(tmix_ready, at(b))
                else:
                    pe.wait_ge(mix_scaled, at(b, 5, j))
                w2, t = (maa_w2[DM * j:DM * (j + 1)], tmix[DM * j:DM * (j + 1)]) if j < 4 else (maa_w2g, tmix_g)
                for ct in range(CT):
                    mm = pe.matmul(PA[:, ct * L:(ct + 1) * L], w2[:, ct * P:(ct + 1) * P], t[:, :],
                                   start=True, stop=True)
                mm.then_inc(mix_mm, 1)

            def columns_product(out, w, rhs, signal):
                for mt in range(CT):
                    for kt in range(CT):
                        mm = pe.matmul(out[:, mt * L:(mt + 1) * L], w[:, kt, mt * P:(mt + 1) * P], rhs[:, kt, :],
                                       start=(kt == 0), stop=(kt == CT - 1))
                mm.then_inc(signal, 1)

            def rows_product(out, w, lhs, signal):
                for t in range(TT):
                    for kt in range(CT):
                        mm = pe.matmul(out[:, t * C:(t + 1) * C], lhs[:, kt, t * P:(t + 1) * P], w[:, kt, :],
                                       start=(kt == 0), stop=(kt == CT - 1))
                mm.then_inc(signal, 1)

            def a_decay(b):
                pe.wait_ge(mix_ready, at(b, 5, 1))
                for kt in range(CT):
                    mm = pe.matmul(PB[0:DD, 0:L], dec_w1[:, kt, :], xmix[:, 0, kt, :], start=(kt == 0), stop=(kt == CT - 1))
                mm.then_inc(proj_mm, 1)

            def a_decay2(b):
                pe.wait_ge(dec_ready, at(b))
                for ct in range(CT):
                    mm = pe.matmul(PB[:, ct * L:(ct + 1) * L], dec_w2[:, ct * P:(ct + 1) * P], dec[:], start=True, stop=True)
                mm.then_inc(dec_mm, 1)

            def a_project(b, j, free):
                pe.wait_ge(mix_ready, at(b, 5, j + 1))
                pe.wait_ge(free, at(b))
                columns_product(PB, sq_w["W" + MIXES[j]], xmix[:, j % 2], proj_mm)

            def a_turn_v(b):
                pe.wait_ge(vT_ready, at(b))
                for t in range(TT):
                    for ct in range(CT):
                        mm = pe.transpose(PB[:, t * C + ct * P:t * C + (ct + 1) * P],
                                          vT[:, ct * L + t * P:ct * L + (t + 1) * P], ident[:])
                mm.then_inc(v_turned, 1)

            def b_chunk(b, g):
                who, n, k = prod_signal(g)
                pe.wait_ge(prod_ready[who], at(b, n, k))
                if g >= 2:
                    pe.wait_ge(av_ready, at(b, N_CHUNKS, g - 1))
                elif g == 0:
                    if later(b):
                        pe.wait_ge(sig_ready, at_before(b))
                pe.matmul(CH[:, (g % 2) * CHUNK:(g % 2 + 1) * CHUNK], ones16[:], prod[:, g % 3, :],
                          start=True, stop=True).then_inc(chunk_mm, 1)

            def b_turn_k(b, lv):
                if lv == 0:
                    pe.wait_ge(av_ready, at(b, N_CHUNKS))
                else:
                    n = sum(1 for g in GROUPS if g[0] < STATES[lv])
                    pe.wait_ge(st_ready, at(b, N_GROUPS, n))
                pe.wait_ge(K_up, at(b, 7, 4 + lv))
                for t in range(TT):
                    for ct in range(CT):
                        mm = pe.transpose(CH[:, t * C + ct * P:t * C + (ct + 1) * P],
                                          K[:, ct * L + t * P:ct * L + (t + 1) * P], ident[:])
                mm.then_inc(k_turned, 1)

            def b_sum(b, n):
                h, tt, q = GROUPS[n]
                lv = STATES.index(h)
                pe.wait_ge(krow_ready, at(b, 8, 2 * lv + 2))
                if n >= 2 and GROUPS[n - 2][0] == h:
                    pe.wait_ge(st_ready, at(b, N_GROUPS, n - 1))
                for ct in range(CT):
                    mm = pe.matmul(CH[:, (n % 2) * 512 + ct * P:(n % 2) * 512 + (ct + 1) * P],
                                   krow[q:q + h, lv % 2, tt, ct * P:(ct + 1) * P],
                                   vrow[q:q + h, tt, ct * P:(ct + 1) * P], start=True, stop=True)
                mm.then_inc(st_mm, 1)

            def b_read(b, n):
                h, tt, q = GROUPS[n]
                R = R_OF[h]
                pe.wait_ge(R_up, at(b, 7, 4 + STATES.index(h)))
                if h > 16:
                    pe.wait_ge(R_kept, at(b, 3, STATES.index(h)))
                if n == 0 and later(b):
                    pe.wait_ge(out_ready, at_before(b))
                if h == P:
                    pe.wait_ge(s0_in, at(b, 16 * P // S))
                    for ct in range(CT):
                        o = ct * L
                        pe.matmul(Y[:, o:o + h], S0[:, ct, :], R[:, o:o + h], start=False, stop=True,
                                  skip_group_check=True)
                pe.wait_ge(st_ready, at(b, N_GROUPS, n + 1))
                lo = tt * P + q + h
                for ct in range(CT):
                    o = ct * L + lo
                    mm = pe.matmul(Y[:, o:o + h], St[:, n % 2, ct, :], R[:, o:o + h],
                                   start=(n == 0 and ct % 2 == 0), stop=(h == P), skip_group_check=True)
                mm.then_inc(y_mm if h == P else st_read, 1)

            def c_mean(b):
                pe.wait_ge(y_ready, at(b))
                pe.wait_ge(st_ready, at(b, N_GROUPS))
                for half in range(2):
                    mm = pe.matmul(CH[:, half * 512:(half + 1) * 512], ones16[:], y[:, half * 512:(half + 1) * 512],
                                   start=True, stop=True)
                mm.then_inc(mean_mm, 1)

            def c_var(b):
                pe.wait_ge(sq_ready, at(b))
                for ct in range(CT):
                    mm = pe.matmul(Y[0:32, 0:L], sel[:, ct, :], sqb[:, ct * L:(ct + 1) * L],
                                   start=(ct == 0), stop=(ct == CT - 1))
                mm.then_inc(var_mm, 1)

            def c_rstd(b):
                pe.wait_ge(grstd_ready, at(b))
                pe.wait_ge(d_ready, at(b))
                for ct in range(CT):
                    mm = pe.matmul(CH[:, ct * L:(ct + 1) * L], selT[:, ct, :], grstd[:], start=True, stop=True)
                mm.then_inc(grstd_mm, 1)

            def c_wo(b):
                pe.wait_ge(yg_ready, at(b))
                rows_product(Y, sq_w["Wo"], cols(y), wo_mm)

            def c_turn(b):
                pe.wait_ge(z2_ready, at(b))
                turn_rows(sqb, CH, z2_turned)

            def c_key(b):
                pe.wait_ge(xk2_ready, at(b))
                columns_product(Y, sq_w["fWk"], xk2, fk_mm)

            def c_receptance(b):
                pe.wait_ge(xr2_ready, at(b))
                rows_product(CH, sq_w["fWr"], xr2, fr_mm)

            def c_value(b):
                pe.wait_ge(kk_ready, at(b))
                rows_product(Y, sq_w["fWv"], cols(sqb), fv_mm)

            def chunks(b, lo, hi):
                if b is not None:
                    for g in range(lo, hi):
                        b_chunk(b, g)

            def states(b, lv):
                if b is None:
                    return
                mine = [n for n in range(N_GROUPS) if GROUPS[n][0] == STATES[lv]]
                for n in mine:
                    b_sum(b, n)
                    if n > mine[0]:
                        b_read(b, n - 1)
                if lv + 1 < len(STATES):
                    b_turn_k(b, lv + 1)
                b_read(b, mine[-1])

            def attention(b):
                a_phi_g(b)
                a_att(b)
                a_theta(b)
                a_wa(b)
                a_x1(b)
                a_turn(b)

            def iteration(a, b, nxt, late):
                A, Bq, N, late_c = a is not None, b is not None, nxt is not None, late is not None
                if A:
                    a_ranks(a)
                chunks(b, 0, 3)
                if A:
                    a_mix(a, 0)
                chunks(b, 3, 5)
                if late_c:
                    c_value(late)
                chunks(b, 5, 8)
                if A:
                    a_mix(a, 1)
                chunks(b, 8, 10)
                if A:
                    a_decay(a)
                chunks(b, 10, 12)
                if A:
                    a_decay2(a)
                chunks(b, 12, N_CHUNKS)
                if A:
                    a_mix(a, 2)
                if Bq:
                    b_turn_k(b, 0)
                for lv in range(len(STATES)):
                    states(b, lv)
                if A:
                    a_project(a, 1, W_ready)
                if Bq:
                    c_mean(b)
                if A:
                    a_mix(a, 3)
                    a_project(a, 2, K_ready)
                if Bq:
                    c_var(b)
                if A:
                    a_mix(a, 4)
                    a_turn_v(a)
                    a_project(a, 3, vrow_ready)
                if Bq:
                    c_rstd(b)
                if N:
                    a_phi_g(nxt)
                if Bq:
                    c_wo(b)
                if A:
                    a_project(a, 4, R_ready)
                if Bq:
                    c_turn(b)
                if N:
                    a_att(nxt)
                    a_theta(nxt)
                    a_wa(nxt)
                if Bq:
                    c_key(b)
                if N:
                    a_x1(nxt)
                if Bq:
                    c_receptance(b)
                if N:
                    a_turn(nxt)

            pe.wait_ge(w_const, 16 * 4)
            pe.wait_ge(ww_scaled, TT)
            for t in range(TT):
                mm = pe.transpose(PB[:, 512 + t * P:512 + (t + 1) * P], ww[:, t, :], ident[:])
            mm.then_inc(ww_turned, 1)
            pe.wait_ge(w_att, 16 * 4)
            pe.wait_ge(wwT_ready, 1)
            attention(0)
            pe.wait_ge(w_mix, 16 * 5)
            for n in SQUARE:
                pe.wait_ge(w_sq[n], 16)
            pe.wait_ge(wo_half, 1)
            iteration(0, None, 1, None)
            iteration(1, 0, 2, None)
            with pe.Fori(2, B - 1) as i:
                iteration(i, i - 1, i + 1, i - 2)
            iteration(B - 1, B - 2, None, B - 3)
            iteration(None, B - 1, None, B - 2)
            c_value(B - 1)

        @block.scalar
        def _(act):
            def a_theta(b):
                act.wait_ge(theta_mm, at(b))
                if later(b):
                    act.wait_ge(x1_mm, at_before(b, TT))
                act.activation(theta[:], PB[:, 0:C], ACT.Identity, bias=theta_b[:, 0:1]).then_inc(theta_ready, 1)

            def a_att(b):
                act.wait_ge(att_mm, at(b))
                act.activation(att[:], PA[:, 0:CI], ACT.Copy, scale=1.0 / C).then_inc(att_ready, 1)

            def a_xa(b):
                act.wait_ge(z1_turned, at(b))
                act.wait_ge(xa0_in, at(b, 16))
                if later(b):
                    act.wait_ge(mix_ready, at_before(b, 5))
                act.activation(xa[:, :, 0:1], xa0[:].unsqueeze(2), ACT.Copy)
                for ct in range(CT):
                    i = act.activation(xa[:, ct, 1:L + 1], PA[:, ct * L:(ct + 1) * L], ACT.Identity,
                                       bias=vec("ln1_b", ct), scale=vec("ln1_w", ct))
                i.then_inc(xa_ready, 1)

            def a_ranks(b):
                act.wait_ge(rank_mm, at(b))
                act.activation(tmix[:], PB[:, 512:768], ACT.Tanh)
                act.activation(tmix_g[:], PB[0:DM, 768:1024], ACT.Tanh).then_inc(tmix_ready, 1)

            def a_decay(b):
                act.wait_ge(proj_mm, at(b, 5, 1))
                act.activation(dec[:], PB[0:DD, 0:L], ACT.Tanh).then_inc(dec_ready, 1)

            def a_decay2(b):
                act.wait_ge(dec_mm, at(b))
                if later(b):
                    act.wait_ge(wprod_ready, at_before(b, 7))
                if later(b):
                    act.wait_ge(R_up, at_before(b, 7, 1))
                if later(b):
                    act.wait_ge(K_up, at_before(b, 7, 1))
                for ct in range(CT):
                    i = act.activation(W[:, ct * L:(ct + 1) * L], PB[:, ct * L:(ct + 1) * L], ACT.Exp,
                                       bias=vec("time_decay", ct))
                i.then_inc(decay_exp, 1)
                act.wait_ge(decay_exp, at(b))
                act.activation(W[:], W[:], ACT.Exp, scale=-1.0).then_inc(W_ready, 1)

            def a_k(b):
                act.wait_ge(proj_mm, at(b, 5, 2))
                if later(b):
                    act.wait_ge(k_turned, at_before(b, 4))
                act.activation(K[:], PB[:], ACT.Copy).then_inc(K_ready, 1)

            def a_v(b):
                act.wait_ge(proj_mm, at(b, 5, 3))
                if later(b):
                    act.wait_ge(av_ready, at_before(b, N_CHUNKS))
                act.activation(vT[:], PB[:], ACT.Copy).then_inc(vT_ready, 1)

            def a_vrow(b):
                act.wait_ge(v_turned, at(b))
                if later(b):
                    act.wait_ge(st_mm, at_before(b, N_GROUPS))
                act.activation(vrow[:].rearrange("p t c -> p (t c)"), PB[:], ACT.Copy).then_inc(vrow_ready, 1)

            def a_r(b):
                act.wait_ge(proj_mm, at(b, 5, 4))
                if later(b):
                    act.wait_ge(y_mm, at_before(b))
                act.activation(RA[:], PB[:], ACT.Copy).then_inc(R_ready, 1)

            def a_g(b):
                act.wait_ge(proj_mm, at(b, 5, 5))
                if later(b):
                    act.wait_ge(yg_ready, at_before(b))
                act.activation(gate[:], PB[:], ACT.Tanh, scale=0.5).then_inc(gtanh_ready, 1)

            def a_keep(b):
                act.wait_ge(x1_ready, at(b, TT))
                if later(b):
                    act.wait_ge(x2_ready, at_before(b))
                act.activation(xres[:], x1[:], ACT.Copy).then_inc(xres_ready, 1)

            def b_krow(b, lv):
                act.wait_ge(k_turned, at(b, 4, lv + 1))
                if lv >= 2:
                    n = sum(1 for g in GROUPS if g[0] <= STATES[lv - 2])
                    act.wait_ge(st_mm, at(b, N_GROUPS, n))
                else:
                    if later(b):
                        act.wait_ge(st_mm, at_before(b, N_GROUPS))
                for t in range(TT):
                    act.activation(krow[:, lv % 2, t, :], CH[:, t * C:(t + 1) * C], ACT.Copy).then_inc(krow_ready, 1)

            def b_keep_r(b, lv):
                h = STATES[lv]
                act.wait_ge(R_up, at(b, 7, 4 + lv))
                if lv:
                    act.wait_ge(R_kept, at(b, 3, lv))
                if lv == 1:
                    act.wait_ge(st_read, at(b, N_GROUPS - 1, sum(1 for g in GROUPS if g[0] == 16)))
                elif lv == 2:
                    act.wait_ge(st_read, at(b, N_GROUPS - 1, sum(1 for g in GROUPS if g[0] <= 32)))
                else:
                    if later(b):
                        act.wait_ge(y_mm, at_before(b))
                act.activation(halves(R_OF[2 * h], h, 0), halves(R_OF[h], h, 0), ACT.Copy).then_inc(R_kept, 1)

            def c_square(b):
                act.wait_ge(d_ready, at(b))
                if later(b):
                    act.wait_ge(fv_mm, at_before(b))
                act.activation(sqb[:], y[:], ACT.Square).then_inc(sq_ready, 1)

            def c_var(b):
                act.wait_ge(var_mm, at(b))
                act.activation(gstd[:], Y[0:32, 0:L], ACT.Sqrt, bias=eps32[:, 0:1]).then_inc(gstd_ready, 1)

            def c_xc(b):
                act.wait_ge(z2_turned, at(b))
                act.wait_ge(xc0_in, at(b, 16))
                if later(b):
                    act.wait_ge(xr2_ready, at_before(b))
                act.activation(xc[:, :, 0:1], xc0[:].unsqueeze(2), ACT.Copy)
                for ct in range(CT):
                    i = act.activation(xc[:, ct, 1:L + 1], CH[:, ct * L:(ct + 1) * L], ACT.Identity,
                                       bias=vec("ln2_b", ct), scale=vec("ln2_w", ct))
                i.then_inc(xc_ready, 1)

            def c_relu(b):
                act.wait_ge(fk_mm, at(b))
                act.activation(sqb[:], Y[:], ACT.Relu).then_inc(relu_ready, 1)

            def c_sig(b):
                act.wait_ge(fr_mm, at(b))
                act.wait_ge(wo_mm, at(b))
                act.activation(y[:], CH[:], ACT.Tanh, scale=0.5).then_inc(sig_ready, 1)

            def attention(b):
                a_att(b)
                a_theta(b)
                a_xa(b)

            def iteration(a, b, nxt, late):
                A, Bq, N, late_c = a is not None, b is not None, nxt is not None, late is not None
                if A:
                    a_ranks(a)
                    a_decay(a)
                    a_decay2(a)
                if Bq:
                    for lv in range(len(STATES)):
                        b_krow(b, lv)
                        if lv < 3:
                            b_keep_r(b, lv)
                if A:
                    a_k(a)
                if Bq:
                    c_square(b)
                if A:
                    a_v(a)
                if Bq:
                    c_var(b)
                if A:
                    a_vrow(a)
                    a_r(a)
                    a_g(a)
                if Bq:
                    c_xc(b)
                if N:
                    a_att(nxt)
                    a_theta(nxt)
                if A:
                    a_keep(a)
                if Bq:
                    c_relu(b)
                    c_sig(b)
                if N:
                    a_xa(nxt)

            act.dma_start(ident[:], ident_d).then_inc(w_const, 16)
            act.dma_start(chan[:], chan_d).then_inc(w_vec, 16)
            act.dma_start(bnv[:], bnv_d).then_inc(w_vec, 16)
            act.dma_start(ww[:], ww_d.rearrange("(t p) c -> p t c", p=P)).then_inc(w_vec, 16)
            act.dma_start(ones16[:], ones16_d).then_inc(w_const, 16)
            act.dma_start(sel[:], sel_d).then_inc(w_const, 16)
            act.dma_start(selT[:], selT_d).then_inc(w_const, 16)
            act.dma_start(maa_w1[:], maa_w1_d.rearrange("(t p) c -> p t c", p=P)).then_inc(w_mix, 16)
            act.dma_start(maa_w2[:], maa_w2_d[0:P]).then_inc(w_mix, 16)
            act.dma_start(maa_w2g[:], maa_w2_d[P:P + DM]).then_inc(w_mix, 16)
            act.dma_start(dec_w1[:], dec_w1_d.rearrange("(t p) c -> p t c", p=P)).then_inc(w_mix, 16)
            act.dma_start(dec_w2[:], dec_w2_d).then_inc(w_mix, 16)
            act.wait_ge(w_vec, 16 * 3)
            act.wait_ge(w_att, 16 * 4)
            act.wait_ge(const_set, 3)
            attention(0)
            iteration(0, None, 1, None)
            iteration(1, 0, 2, None)
            with act.Fori(2, B - 1) as i:
                iteration(i, i - 1, i + 1, i - 2)
            iteration(B - 1, B - 2, None, B - 3)
            iteration(None, B - 1, None, B - 2)

        @block.vector
        def _(dve):
            def layer_norm_stats(src, b, st, agg, stat_sem, aggr_sem, ready, steps):
                for t in range(TT):
                    dve.wait_ge(ready, at(b, steps, t + 1 if steps > 1 else 1))
                    dve.bn_stats(st[:, t, :], src[:, t, :]).then_inc(stat_sem, 1)
                dve.drain()
                for t in range(TT):
                    dve.bn_aggr(agg[:, t, :], st[:, t, :]).then_inc(aggr_sem, 1)

            def a_phi_g(b):
                dve.wait_ge(pg_mm, at(b))
                dve.tensor_tensor(zbuf[:].rearrange("p (m c) -> p m c", m=CT), PA[:].rearrange("p (m c) -> p m c", m=CT),
                                  pg_bias[:].unsqueeze(1).to_broadcast([P, CT, 2 * CI]), ALU.add).then_inc(pg_ready, 1)

            def a_wa(b):
                dve.wait_ge(wa_mm, at(b))
                dve.tensor_copy(wa[:], PA[:, 512:512 + L]).then_inc(wa_ready, 1)

            def a_x1(b):
                if later(b):
                    dve.wait_ge(xres_ready, at_before(b))
                for t in range(TT):
                    dve.wait_ge(x1_mm, at(b, TT, t + 1))
                    dve.scalar_tensor_tensor(x1[:, t, :], PA[:, t * C:(t + 1) * C], bn_t[:, t:t + 1], x[:, t, :],
                                             ALU.add, ALU.add).then_inc(x1_ready, 1)
                layer_norm_stats(x1, b, stats, mv, bn1_stat, bn1_aggr, x1_ready, TT)

            def a_z(b):
                dve.wait_ge(rstd1_ready, at(b))
                for t in range(TT):
                    i = dve.tensor_scalar(zbuf[:, t * C:(t + 1) * C], x1[:, t, :], mv[:, t, 0:1], rstd[:, t:t + 1],
                                          ALU.subtract, ALU.mult)
                i.then_inc(z1_ready, 1)

            def a_shift(b):
                dve.wait_ge(xa_ready, at(b))
                dve.tensor_tensor(sx[:], xa[:, :, 0:L], xa[:, :, 1:L + 1], ALU.subtract).then_inc(sx_ready, 1)
                dve.wait_ge(sx_ready, at(b))
                for ct in range(CT):
                    i = dve.scalar_tensor_tensor(zbuf[:, ct * L:(ct + 1) * L], sx[:, ct, :], vec("maa_x", ct),
                                                 xa[:, ct, 1:L + 1], ALU.mult, ALU.add)
                i.then_inc(xxx_ready, 1)

            def a_mix(b, j):
                dve.wait_ge(mix_mm, at(b, 5, j + 1))
                if j >= 2:
                    dve.wait_ge(proj_mm, at(b, 5, j - 1))
                else:
                    if later(b):
                        dve.wait_ge(proj_mm, at_before(b, 5, 5 if j == 0 else 4))
                for ct in range(CT):
                    i = dve.scalar_tensor_tensor(xmix[:, j % 2, ct, :], PA[:, ct * L:(ct + 1) * L],
                                                 vec("maa_" + MIXES[j], ct), sx[:, ct, :], ALU.add, ALU.mult)
                i.then_inc(mix_scaled, 1)

            def a_gate(b):
                dve.wait_ge(gtanh_ready, at(b))
                dve.scalar_tensor_tensor(gate[:], gate[:], 1.0, PB[:], ALU.add, ALU.mult).then_inc(gate_ready, 1)

            def b_prod(b, g):
                _, h, c = CHUNKS[g]
                if g >= 3:
                    dve.wait_ge(chunk_mm, at(b, N_CHUNKS, g - 2))
                else:
                    if later(b):
                        dve.wait_ge(chunk_mm, at_before(b, N_CHUNKS))
                if h == 0:
                    dve.wait_ge(K_ready, at(b))
                    dve.wait_ge(R_ready, at(b))
                    for half in range(2):
                        ct = 2 * c + half
                        i = dve.scalar_tensor_tensor(prod[:, g % 3, half * L:(half + 1) * L], RA[:, ct * L:(ct + 1) * L],
                                                     vec("faaaa", ct), K[:, ct * L:(ct + 1) * L], ALU.mult, ALU.mult)
                else:
                    nb = CHUNK // (h * h)
                    if h > 1:
                        dve.wait_ge(R_up, at(b, 7, INTRA.index(h)))
                        dve.wait_ge(K_up, at(b, 7, INTRA.index(h)))
                    r = pairs(RA[:], h, c, 1).unsqueeze(3).to_broadcast([P, nb, h, h])
                    k = pairs(K[:], h, c, 0).unsqueeze(2).to_broadcast([P, nb, h, h])
                    i = dve.tensor_tensor(by_pair(prod[:, g % 3, :], h), r, k, ALU.mult)
                i.then_inc(prod_ready["dve"], 1)

            N_RED = sum(1 for _, h, c in CHUNKS if h > 1)

            def b_weigh(b, g):
                _, h, c = CHUNKS[g]
                src = CH[:, (g % 2) * CHUNK:(g % 2 + 1) * CHUNK]
                dve.wait_ge(chunk_mm, at(b, N_CHUNKS, g + 1))
                if h == 0:
                    if g == 0:
                        dve.wait_ge(vT_ready, at(b))
                        if later(b):
                            dve.wait_ge(y_ready, at_before(b))
                    dve.tensor_tensor(yint[:, c * CHUNK:(c + 1) * CHUNK], src, vT[:, c * CHUNK:(c + 1) * CHUNK],
                                      ALU.mult).then_inc(av_ready, 1)
                    return
                nb = CHUNK // (h * h)
                v = pairs(vT[:], h, c, 0).unsqueeze(2).to_broadcast([P, nb, h, h])
                dst = yred[:] if h == 1 else av[:, g % 2, :]
                if h == 1:
                    if later(b):
                        dve.wait_ge(yint_ready, at_before(b, len(INTRA)))
                elif g >= FIRST_CHUNK[2] + 2:
                    dve.wait_ge(red_ready, at(b, N_RED, g - 1 - FIRST_CHUNK[2]))
                dve.tensor_tensor(by_pair(dst, h), by_pair(src, h), v, ALU.mult).then_inc(av_ready, 1)
                dve.wait_ge(av_ready, at(b, N_CHUNKS, g + 1))
                if h > 1:
                    n = CHUNK // h
                    if c == 0:
                        dve.wait_ge(yint_ready, at(b, len(INTRA), INTRA.index(h)))
                    dve.tensor_reduce(yred[:, c * n:(c + 1) * n], by_pair(dst, h), AX.X, ALU.add).then_inc(red_ready, 1)
                if c == h - 1:
                    if h > 1:
                        dve.wait_ge(red_ready, at(b, N_RED, g + 1 - FIRST_CHUNK[2]))
                    o = halves(yint[:], h, 1)
                    dve.tensor_tensor(o, o, yred[:].rearrange("p (n h) -> p n h", h=h), ALU.add).then_inc(yint_ready, 1)

            def b_wprod(b):
                for n, h in enumerate([1, 2, 4, 8, 16, 32, 64]):
                    if h == 1:
                        dve.wait_ge(W_ready, at(b))
                        if later(b):
                            dve.wait_ge(st_ready, at_before(b, N_GROUPS))
                    w = wblocks(h)
                    i = dve.tensor_tensor(wprod[:, WOFF[2 * h]:WOFF[2 * h] + F // (2 * h)].unsqueeze(2), w[:, :, 0:1],
                                          w[:, :, 1:2], ALU.mult)
                    i.then_inc(wprod_ready, 1)
                    dve.wait_ge(wprod_ready, at(b, 7, n + 1))

            def b_update_r(b, h):
                n = [1, 2, 4, 8, 16, 32, 64].index(h)
                if h == 1:
                    dve.wait_ge(W_ready, at(b))
                if h < 16:
                    src = dst = RA
                    if h > 1:
                        dve.wait_ge(prod_ready["pool"], at(b, len(POOL_CHUNKS), sum(1 for g in POOL_CHUNKS if CHUNKS[g][1] <= h)))
                    dve.wait_ge(prod_ready["dve"], at(b, len(DVE_CHUNKS), sum(1 for g in DVE_CHUNKS if CHUNKS[g][1] <= h)))
                else:
                    src, dst = R_OF[h], R_OF[2 * h]
                    if h == 32:
                        dve.wait_ge(st_read, at(b, N_GROUPS - 1, sum(1 for g in GROUPS if g[0] == 16)))
                    if h == 64:
                        dve.wait_ge(st_read, at(b, N_GROUPS - 1, sum(1 for g in GROUPS if g[0] <= 32)))
                    if h > 16:
                        dve.wait_ge(R_kept, at(b, 3, n - 4))
                    dve.wait_ge(R_up, at(b, 7, n))
                dve.tensor_tensor(halves(dst[:], h, 1), halves(src[:], h, 1), wfactor(h, 0), ALU.mult).then_inc(R_up, 1)

            def b_mask(b, n):
                h, tt, q = GROUPS[n]
                dve.wait_ge(st_mm, at(b, N_GROUPS, n + 1))
                if n >= 2:
                    dve.wait_ge(st_read, at(b, N_GROUPS - 1, n - 1))
                else:
                    if later(b):
                        dve.wait_ge(y_mm, at_before(b))
                i = dve.tensor_tensor(St[:, n % 2], CH[:, (n % 2) * 512:(n % 2 + 1) * 512].rearrange(
                    "p (c k) -> p c k", c=CT), ones16[:].unsqueeze(1).to_broadcast([P, CT, P]), ALU.mult)
                if h < P:
                    i.then_inc(st_ready, 1)
                    return
                i.then_inc(s1_masked, 1)
                dve.wait_ge(s1_masked, at(b))
                dve.wait_ge(s0_in, at(b, 16 * P // S))
                for ct in range(CT):
                    i = dve.scalar_tensor_tensor(St[:, n % 2, ct, :], S0[:, ct, :], wprod[:, WOFF[P] + 2 * ct:WOFF[P] + 2 * ct + 1],
                                                 St[:, n % 2, ct, :], ALU.mult, ALU.add)
                i.then_inc(st_ready, 1)

            def b_y(b):
                dve.wait_ge(y_mm, at(b))
                dve.wait_ge(yint_ready, at(b, len(INTRA)))
                if later(b):
                    dve.wait_ge(ff_scaled, at_before(b))
                dve.tensor_tensor(y[:], Y[:], yint[:], ALU.add).then_inc(y_ready, 1)

            def c_center(b):
                dve.wait_ge(mean_mm, at(b))
                dve.wait_ge(y_ready, at(b))
                dve.scalar_tensor_tensor(y[:], CH[:], -1.0 / S, y[:], ALU.mult, ALU.add).then_inc(d_ready, 1)

            def c_grstd(b):
                dve.wait_ge(gstd_ready, at(b))
                if later(b):
                    dve.wait_ge(grstd_mm, at_before(b))
                dve.reciprocal(grstd[:], gstd[:]).then_inc(grstd_ready, 1)

            def c_gate(b):
                dve.wait_ge(grstd_mm, at(b))
                dve.wait_ge(sq_ready, at(b))
                for ct in range(CT):
                    c = slice(ct * L, (ct + 1) * L)
                    i = dve.scalar_tensor_tensor(y[:, c], y[:, c], vec("gn_w", ct), CH[:, c], ALU.mult, ALU.mult)
                i.then_inc(yn_ready, 1)
                dve.wait_ge(yn_ready, at(b))
                for ct in range(CT):
                    c = slice(ct * L, (ct + 1) * L)
                    i = dve.scalar_tensor_tensor(y[:, c], y[:, c], vec("gn_b", ct), gate[:, c], ALU.add, ALU.mult)
                i.then_inc(yg_ready, 1)

            def c_x2(b):
                dve.wait_ge(wo_mm, at(b))
                dve.wait_ge(xres_ready, at(b))
                if later(b):
                    dve.wait_ge(out_stored, at_before(b, 16))
                dve.tensor_tensor(x2[:].rearrange("p t c -> p (t c)"), Y[:], xres[:].rearrange("p t c -> p (t c)"),
                                  ALU.add).then_inc(x2_ready, 1)
                layer_norm_stats(x2, b, stats2, mv2, bn2_stat, bn2_aggr, x2_ready, 1)

            def c_z(b):
                dve.wait_ge(rstd2_ready, at(b))
                dve.wait_ge(var_mm, at(b))
                for t in range(TT):
                    i = dve.tensor_scalar(sqb[:, t * C:(t + 1) * C], x2[:, t, :], mv2[:, t, 0:1], rstd2[:, t:t + 1],
                                          ALU.subtract, ALU.mult)
                i.then_inc(z2_ready, 1)

            def c_shift(b):
                dve.wait_ge(xc_ready, at(b))
                dve.tensor_tensor(sxc, xc[:, :, 0:L], xc[:, :, 1:L + 1], ALU.subtract).then_inc(sxc_ready, 1)
                dve.wait_ge(sxc_ready, at(b))
                for name, dst, signal, used in [("fmaa_k", xk2, xk2_ready, fk_mm), ("fmaa_r", xr2, xr2_ready, fr_mm)]:
                    if later(b):
                        dve.wait_ge(used, at_before(b))
                    for ct in range(CT):
                        i = dve.scalar_tensor_tensor(dst[:, ct, :], sxc[:, ct, :], vec(name, ct), xc[:, ct, 1:L + 1],
                                                     ALU.mult, ALU.add)
                    i.then_inc(signal, 1)

            def c_out(b):
                dve.wait_ge(fv_mm, at(b))
                dve.wait_ge(sig_ready, at(b))
                dve.scalar_tensor_tensor(y[:], y[:], 1.0, Y[:], ALU.add, ALU.mult).then_inc(ff_scaled, 1)
                dve.wait_ge(ff_scaled, at(b))
                x2f = x2[:].rearrange("p t c -> p (t c)")
                dve.scalar_tensor_tensor(x2f, y[:], 0.5, x2f, ALU.mult, ALU.add).then_inc(out_ready, 1)

            def chunks(b, lo, hi):
                if b is None:
                    return
                for g in range(lo, hi):
                    h = CHUNKS[g][1]
                    if g == 1:
                        b_wprod(b)
                    nxt = g + 2
                    if nxt < N_CHUNKS:
                        if CHUNKS[nxt][1] > 1 and CHUNKS[nxt - 1][1] != CHUNKS[nxt][1]:
                            b_update_r(b, CHUNKS[nxt - 1][1])
                        if nxt in DVE_CHUNKS:
                            b_prod(b, nxt)
                    elif nxt == N_CHUNKS:
                        b_update_r(b, 8)
                    b_weigh(b, g)

            def states(b):
                if b is None:
                    return
                for n in range(N_GROUPS):
                    h = GROUPS[n][0]
                    if h < P and (n == 0 or GROUPS[n - 1][0] != h):
                        b_update_r(b, h) if h == 16 else None
                    b_mask(b, n)
                    if h < 64 and GROUPS[n + 1][0] != h:
                        b_update_r(b, 2 * h)
                b_y(b)

            def attention(b):
                a_phi_g(b)
                a_wa(b)
                a_x1(b)
                a_z(b)

            def iteration(a, b, nxt, late):
                A, Bq, N, late_c = a is not None, b is not None, nxt is not None, late is not None
                if Bq:
                    b_prod(b, 0)
                    b_prod(b, 1)
                chunks(b, 0, 3)
                if A:
                    a_mix(a, 0)
                chunks(b, 3, 8)
                if late_c:
                    c_out(late)
                if A:
                    a_mix(a, 1)
                chunks(b, 8, N_CHUNKS)
                if A:
                    a_mix(a, 2)
                states(b)
                if Bq:
                    c_center(b)
                if A:
                    a_mix(a, 3)
                if Bq:
                    c_grstd(b)
                if A:
                    a_mix(a, 4)
                if Bq:
                    c_gate(b)
                if N:
                    a_phi_g(nxt)
                if Bq:
                    c_x2(b)
                    c_z(b)
                if A:
                    a_gate(a)
                if Bq:
                    c_shift(b)
                if N:
                    a_wa(nxt)
                    a_x1(nxt)
                    a_z(nxt)
                    a_shift(nxt)

            dve.memset(eps_c[:], EPS).then_inc(const_set, 1)
            dve.memset(neg_half[:], -0.5).then_inc(const_set, 1)
            dve.memset(eps32[:], EPS).then_inc(const_set, 1)
            dve.memset(S0[:], 0.0).then_inc(s0_zero, 1)
            W_B, GAMMA, BETA, MEAN = 0, 1, 2, 3
            dve.wait_ge(bn_ready, 1)
            for t in range(TT):
                dve.tensor_scalar(ww[:, t, :], ww[:, t, :], bn_s[:, t:t + 1], None, ALU.mult).then_inc(ww_scaled, 1)
            dve.wait_ge(w_vec, 48)
            dve.tensor_tensor(bn_tmp[:, 1, :], bnv[:, W_B, :], bnv[:, MEAN, :], ALU.subtract).then_inc(ww_scaled, 1)
            dve.wait_ge(ww_scaled, TT + 1)
            dve.tensor_tensor(bn_tmp[:, 1, :], bn_tmp[:, 1, :], bn_s[:], ALU.mult).then_inc(ww_scaled, 1)
            dve.wait_ge(ww_scaled, TT + 2)
            dve.tensor_tensor(bn_t[:], bn_tmp[:, 1, :], bnv[:, BETA, :], ALU.add).then_inc(ww_scaled, 1)
            dve.wait_ge(ww_scaled, TT + 3)
            dve.wait_ge(ww_turned, 1)
            dve.tensor_copy(wwT[:], PB[:, 512:512 + L]).then_inc(wwT_ready, 1)
            dve.wait_ge(w_att, 64)
            attention(0)
            a_shift(0)
            dve.wait_ge(w_sq["Wo"], 16)
            dve.tensor_scalar(sq_w["Wo"][:], sq_w["Wo"][:], 0.5, None, ALU.mult).then_inc(wo_half, 1)
            iteration(0, None, 1, None)
            iteration(1, 0, 2, None)
            with dve.Fori(2, B - 1) as i:
                iteration(i, i - 1, i + 1, i - 2)
            iteration(B - 1, B - 2, None, B - 3)
            iteration(None, B - 1, None, B - 2)
            c_out(B - 1)

        @block.gpsimd
        def _(pool):
            def a_rstd(b):
                pool.wait_ge(bn1_aggr, at(b, TT))
                pool.tensor_tensor(mv[:, :, 1], mv[:, :, 1], eps_c[:], ALU.add).then_inc(var1_eps, 1)
                pool.wait_ge(var1_eps, at(b))
                if later(b):
                    pool.wait_ge(z1_ready, at_before(b))
                pool.tensor_tensor(rstd[:], mv[:, :, 1], neg_half[:], ALU.pow).then_inc(rstd1_ready, 1)

            def a_mix(b, j):
                pool.wait_ge(mix_scaled, at(b, 5, j + 1))
                m = xmix[:, j % 2]
                pool.tensor_tensor(m, m, xa[:, :, 1:L + 1], ALU.add).then_inc(mix_ready, 1)

            def b_prod(b, g):
                _, h, c = CHUNKS[g]
                nb = CHUNK // (h * h)
                pool.wait_ge(chunk_mm, at(b, N_CHUNKS, g - 2))
                pool.wait_ge(R_up, at(b, 7, INTRA.index(h)))
                pool.wait_ge(K_up, at(b, 7, INTRA.index(h)))
                r = pairs(RA[:], h, c, 1).unsqueeze(3).to_broadcast([P, nb, h, h])
                k = pairs(K[:], h, c, 0).unsqueeze(2).to_broadcast([P, nb, h, h])
                pool.tensor_tensor(by_pair(prod[:, g % 3, :], h), r, k, ALU.mult).then_inc(prod_ready["pool"], 1)

            def b_update_k(b, h):
                n = [1, 2, 4, 8, 16, 32, 64].index(h)
                if h == 1:
                    pool.wait_ge(W_ready, at(b))
                    pool.wait_ge(K_ready, at(b))
                if h == 2:
                    pool.wait_ge(wprod_ready, at(b, 7))
                if h <= 8:
                    pool.wait_ge(prod_ready["dve"], at(b, len(DVE_CHUNKS), sum(1 for g in DVE_CHUNKS if CHUNKS[g][1] <= h)))
                    if h > 1:
                        pool.wait_ge(prod_ready["pool"], at(b, len(POOL_CHUNKS), sum(1 for g in POOL_CHUNKS if CHUNKS[g][1] <= h)))
                else:
                    pool.wait_ge(k_turned, at(b, 4, n - 3))
                    pool.wait_ge(K_up, at(b, 7, n))
                ke = halves(K[:], h, 0)
                pool.tensor_tensor(ke, ke, wfactor(h, 1), ALU.mult).then_inc(K_up, 1)

            def c_rstd(b):
                pool.wait_ge(bn2_aggr, at(b, TT))
                pool.tensor_tensor(mv2[:, :, 1], mv2[:, :, 1], eps_c[:], ALU.add).then_inc(var2_eps, 1)
                pool.wait_ge(var2_eps, at(b))
                if later(b):
                    pool.wait_ge(z2_ready, at_before(b))
                pool.tensor_tensor(rstd2[:], mv2[:, :, 1], neg_half[:], ALU.pow).then_inc(rstd2_ready, 1)

            def c_square(b):
                pool.wait_ge(relu_ready, at(b))
                pool.tensor_tensor(sqb[:], sqb[:], sqb[:], ALU.mult).then_inc(kk_ready, 1)

            def chunks(b, lo, hi):
                if b is None:
                    return
                for g in range(lo, hi):
                    nxt = g + 2
                    if nxt < N_CHUNKS:
                        if CHUNKS[nxt][1] > 1 and CHUNKS[nxt - 1][1] != CHUNKS[nxt][1]:
                            b_update_k(b, CHUNKS[nxt - 1][1])
                        if nxt in POOL_CHUNKS:
                            b_prod(b, nxt)
                    elif nxt == N_CHUNKS:
                        b_update_k(b, 8)

            def attention(b):
                a_rstd(b)

            def iteration(a, b, nxt, late):
                A, Bq, N, late_c = a is not None, b is not None, nxt is not None, late is not None
                chunks(b, 0, 3)
                if A:
                    a_mix(a, 0)
                chunks(b, 3, 8)
                if A:
                    a_mix(a, 1)
                chunks(b, 8, N_CHUNKS)
                if A:
                    a_mix(a, 2)
                if Bq:
                    for h in [16, 32, 64]:
                        b_update_k(b, h)
                if A:
                    a_mix(a, 3)
                    a_mix(a, 4)
                if Bq:
                    c_rstd(b)
                    c_square(b)
                if N:
                    a_rstd(nxt)

            GAMMA, VAR = 1, 4
            pool.wait_ge(const_set, 3)
            pool.wait_ge(w_vec, 48)
            pool.tensor_tensor(bn_tmp[:, 0, :], bnv[:, VAR, :], eps_c[:], ALU.add).then_inc(pool_set, 1)
            pool.wait_ge(pool_set, 1)
            pool.tensor_tensor(bn_s[:], bn_tmp[:, 0, :], neg_half[:], ALU.pow).then_inc(pool_set, 1)
            pool.wait_ge(pool_set, 2)
            pool.tensor_tensor(bn_s[:], bn_s[:], bnv[:, GAMMA, :], ALU.mult).then_inc(bn_ready, 1)
            attention(0)
            iteration(0, None, 1, None)
            iteration(1, 0, 2, None)
            with pool.Fori(2, B - 1) as i:
                iteration(i, i - 1, i + 1, i - 2)
            iteration(B - 1, B - 2, None, B - 3)
            iteration(None, B - 1, None, B - 2)


def kernel(**inputs):
    import numpy as np
    import concourse.bacc as bacc
    from concourse.bass_utils import run_bass_kernel_spmd

    B, L, C = inputs["x"].shape
    S = 16
    a0 = {k[len("L0_xattn_"):]: np.asarray(v) for k, v in inputs.items() if k.startswith("L0_xattn_")}
    a1 = {k[len("L1_xattn_"):]: np.asarray(v) for k, v in inputs.items() if k.startswith("L1_xattn_")}
    ctx = np.asarray(inputs["ctx_2048"])
    head = np.arange(P) // S
    tile_head = np.arange(C).reshape(C // P, P) // S
    sel = (tile_head[:, :, None] == np.arange(C // S)).astype(np.float32)
    arrays = {
        "x": np.asarray(inputs["x"]),
        "ctx": ctx,
        "shift": ctx[:, 0:2, :].reshape(B, 2, C // P, P).transpose(0, 1, 3, 2),
        "chan": np.stack([a1[n].reshape(C // P, P).T for n in CHANNEL_VECTORS], axis=1),
        "bnv": np.stack([a0[n].reshape(L // P, P).T for n in BN_VECTORS], axis=1),
        "theta_b": a0["theta_b"].reshape(P, 1),
        "pg_bias": np.concatenate([a0["phi_b"], a0["g_b"]]),
        "thetaT": a0["theta_w"].T,
        "pgT": np.concatenate([a0["phi_w"].T, a0["g_w"].T], axis=1),
        "ww": a0["w_w"],
        "maa_w1": a1["maa_w1"],
        "maa_w2": a1["maa_w2"].reshape(-1, C),
        "dec_w1": a1["decay_w1"],
        "dec_w2": a1["decay_w2"],
        "square": np.stack([a1[n].T for n in SQUARE]),
        "ident": np.eye(P, dtype=np.float32),
        "ones16": (head[:, None] == head[None, :]).astype(np.float32),
        "sel": sel.transpose(1, 0, 2) / np.float32(S),
        "selT": sel.transpose(2, 0, 1),
    }
    nc = bacc.Bacc("TRN2", target_bir_lowering=False, num_devices=1)
    feed, args = {}, []
    for name, a in arrays.items():
        a = np.ascontiguousarray(a)
        feed["in_" + name] = a
        args.append(nc.dram_tensor("in_" + name, a.shape, mybir.dt.from_np(a.dtype), kind="ExternalInput").ap())
    args.append(nc.dram_tensor("out_x", (B, L, C), F32, kind="ExternalOutput").ap())
    build_xattn_rwkv(nc, *args)
    r = run_bass_kernel_spmd(nc, [feed], core_ids=[0])
    return r.results[0]["out_x"]
```
